# Optimizing a Trainium2 kernel written in Bass

```python
import numpy as np
import jax
import jax.numpy as jnp

def _softmax(x, axis=-1):
    return jax.nn.softmax(x, axis=axis)

def _gelu(x):
    return jax.nn.gelu(x, approximate=True)

def _silu(x):
    return jax.nn.silu(x)

def _sigmoid(x):
    return jax.nn.sigmoid(x)

def _layernorm(x, axis=-1, eps=1e-05):
    m = jnp.mean(x, axis=axis, keepdims=True)
    v = jnp.var(x, axis=axis, keepdims=True)
    return (x - m) / jnp.sqrt(v + eps)

def _scatter_add(tgt, idx, src, axis=0):
    return tgt.at[idx].add(src)

def _segment_sum(src, seg, n):
    return jax.ops.segment_sum(src, seg, n)
kernel_name = 'mk_adj_preln_d1_adj_r2_3937d6'

def setup_inputs(seed: int=0):
    np.random.seed(seed)
    _w = jnp.asarray

    def _rec_inputs():
        import jax
        import jax.numpy as jnp
        _gk = jax.random.key(seed)
        x = 7.22e-05 + 1 * jax.random.normal(jax.random.fold_in(_gk, 1), (8, 2048, 128), jnp.float32)
        _a = jax.random.bernoulli(jax.random.fold_in(_gk, 2), 0.000976562, (2048, 2048))
        _a = jnp.logical_or(_a, jnp.swapaxes(_a, -1, -2))
        _a = jnp.logical_or(_a, jnp.eye(2048, dtype=bool))
        _af = _a.astype(jnp.float32)
        _af = _af * jax.random.uniform(jax.random.fold_in(_gk, 3), (2048, 2048), jnp.float32, 0.05, 0.119748)
        adj = _af
        return (x, adj)
    x, adj = _rec_inputs()

    def _L0_gnn_setup():
        import jax, jax.numpy as jnp
        import numpy as np
        B, N, F_IN, F_OUT = (8, 2048, 128, 128)
        key = jax.random.key(seed)
        k1, k2, k3 = jax.random.split(key, 3)
        H = jax.random.normal(k1, (B, N, F_IN), dtype=jnp.float32)
        W = jax.random.normal(k2, (F_IN, F_OUT), dtype=jnp.float32) * (1.0 / np.sqrt(F_IN))
        A = jax.random.normal(k3, (N, N), dtype=jnp.float32) * (1.414 * np.sqrt(2.0 / (N + N)))
        return {'H': H, 'W': W, 'A': A}
    _L0_gnn_all = _L0_gnn_setup()
    _L0_gnn_in = {k: v for k, v in _L0_gnn_all.items() if k in ('W',)}
    del _L0_gnn_all
    return {'x': x, 'adj': adj, 'L0_gnn_W': _L0_gnn_in['W']}

def reference(x, adj, L0_gnn_W):
    import jax
    import jax.numpy as jnp

    def _L0_gnn_ref(H, W, A):
        import jax, jax.numpy as jnp
        import numpy as np
        B, N, F_IN, F_OUT = (8, 2048, 128, 128)
        HW = jnp.einsum('bnf,fo->bno', H, W)
        A_norm = jax.nn.relu((A + A.T) * 0.5)
        D = jnp.sum(A_norm, axis=1)
        D_safe = jnp.where(D > 0, D, 1.0)
        d_inv_sqrt = jnp.where(D > 0, D_safe ** (-0.5), 0.0)
        DAD = d_inv_sqrt[:, None] * A_norm * d_inv_sqrt[None, :]
        L_norm = jnp.eye(N, dtype=H.dtype) - DAD
        out = jnp.einsum('nm,bmo->bno', L_norm, HW)
        return jax.nn.relu(out)
    h = jnp.maximum(_layernorm(x, axis=-1), 0.0)
    x = x + _L0_gnn_ref(h, L0_gnn_W, adj)
    return x

_drawn_inputs = setup_inputs


def setup_inputs(seed=0):
    import zlib

    import numpy as np

    out = dict(_drawn_inputs(seed))
    spreads = {}
    factors = {}
    for name, (base, spread) in spreads.items():
        noise = np.random.default_rng([zlib.crc32(name.encode()), seed]).standard_normal(out[name].shape)
        drawn = base * np.exp(spread * noise) if base else spread * noise
        out[name] = jnp.asarray(drawn.astype(out[name].dtype))
    for name, factor in factors.items():
        out[name] = (out[name] * factor).astype(out[name].dtype)
    return out
```

```python
from contextlib import ExitStack

import concourse.bass as bass
from concourse import mybir
from concourse.alu_op_type import AluOpType as ALU

F32 = mybir.dt.float32
F16 = mybir.dt.float16
U32 = mybir.dt.uint32
ACT = mybir.ActivationFunctionType
AX_X = mybir.AxisListType.X

P = 128
GRP = 4
WIDE = GRP * P
EPS = 1e-5
L_SCALE = 2.0 ** 14
H_SCALE = 2.0 ** 10
X_SLOTS = 3
TMP_SLOTS = 3
LEAD = 3


def gnn_layer(nc, x, adj, w, out):
    B, N, F = x.shape
    T = N // P
    G = T // GRP
    HALVES = B // GRP
    NEPI = HALVES * T

    jobs = []
    for n in range(T):
        for g in range(n // GRP):
            jobs.append(("pair", n, g))
        if n % GRP == GRP - 1:
            jobs += [("diag", n // GRP, 0), ("diag", n // GRP, 1)]
    jobs_of_row = [[j for j, job in enumerate(jobs)
                    if (job[1] if job[0] == "pair" else job[1] * GRP + GRP - 1) == n] for n in range(T)]
    relu_units = []
    for n in range(T):
        grp = n // GRP
        for j in jobs_of_row[n]:
            kind, a, b = jobs[j]
            if kind == "pair":
                relu_units.append((n, n, b, 2 * j + 1))
                if n % GRP == GRP - 1:
                    relu_units += [(n, GRP * b + i, grp, 2 * j + 2) for i in range(GRP)]
            else:
                relu_units += [(n, GRP * a + 2 * b + i, a, 2 * j + 1 + i) for i in range(2)]
    n_units = len(relu_units)
    XPLAN = [2] + [1] * (T - 2) + [0]
    xunits_after_row, u = [], 0
    for k in XPLAN:
        xunits_after_row.append(list(range(u, u + k)))
        u += k
    assert u == T

    x_v = x.rearrange("(h b) (t p) f -> h t p b f", b=GRP, p=P)
    out_v = out.rearrange("(h b) (t p) f -> h t p b f", b=GRP, p=P)
    adj_v = adj.rearrange("(t p) m -> t p m", p=P)

    with ExitStack() as ctx:
        def sb(name, shape, dt=F32):
            return ctx.enter_context(nc.sbuf_tensor(name, shape, dt))

        def sem(name):
            return ctx.enter_context(nc.semaphore(name))

        S = sb("S", [P, T, N])
        L16 = S[:].bitcast(F16)
        hw_hi = sb("hw_hi", [P, HALVES, T, WIDE], F16)
        hw_lo = sb("hw_lo", [P, HALVES, T, WIDE], F16)
        xin = sb("xin", [P, X_SLOTS, WIDE])
        hT = sb("hT", [P, 2, WIDE])
        tmp = sb("tmp", [P, TMP_SLOTS, WIDE])
        drow = sb("drow", [P, WIDE])
        xres = sb("xres", [P, 2, WIDE])
        res = sb("res", [P, 2, WIDE])
        ident = sb("ident", [P, P])
        ident_s = sb("ident_s", [P, P])
        w_sb = sb("w_sb", [P, P])
        svec = sb("svec", [P, P])
        stats = sb("stats", [P, 2, GRP, 6])
        mv = sb("mv", [P, 2, GRP, 2])
        lnt = sb("lnt", [P, 2, 4, GRP])
        mhalf = sb("mhalf", [P, T])
        deg_part = sb("deg_part", [P, T, G])
        deg = sb("deg", [P, 6, T])
        dcol = sb("dcol", [P, T])
        ndcol = sb("ndcol", [P, T])
        ones = xres[:, 0, 0:P]
        w_abs = xres[:, 0, P:2 * P]
        w_raw = xres[:, 0, 2 * P:3 * P]
        w_inv = xres[:, 0, 3 * P:4 * P]
        w_sum = xres[:, 1, 0:P]
        ps = ctx.enter_context(nc.psum_tensor("ps", [P, 8, WIDE], F32))

        adj_in = [sem(f"adj_in{n}") for n in range(T)]
        w_in = sem("w_in")
        x_in = [sem(f"x_in{s}") for s in range(X_SLOTS)]
        res_in = [sem(f"res_in{s}") for s in range(2)]
        out_done = [sem(f"out_done{s}") for s in range(2)]
        ident_zero = sem("ident_zero")
        ident_ready = sem("ident_ready")
        consts_ready = sem("consts_ready")
        w_chain = sem("w_chain")
        w_summed = sem("w_summed")
        w_ready = sem("w_ready")
        a_turned = sem("a_turned")
        a_added = sem("a_added")
        unit_relu = sem("unit_relu")
        deg_summed = sem("deg_summed")
        deg_chain = sem("deg_chain")
        d_ready = sem("d_ready")
        stats_raw = sem("stats_raw")
        stats_ready = sem("stats_ready")
        ln_chain = sem("ln_chain")
        xn_ready = sem("xn_ready")
        t_turned = sem("t_turned")
        t_taken = sem("t_taken")
        hw_done = sem("hw_done")
        hw_hi_ready = sem("hw_hi_ready")
        hw_lo_ready = sem("hw_lo_ready")
        l_scaled = sem("l_scaled")
        l_diag = sem("l_diag")
        l_hi_ready = sem("l_hi_ready")
        l_lo_ready = sem("l_lo_ready")
        prod_done = sem("prod_done")
        prod_taken = sem("prod_taken")
        res_ready = sem("res_ready")

        tjobs = [("x", u) for u in range(T)]
        for g in range(G):
            tjobs.append(("drow", g))
            tjobs += [("x", T + 4 * g + i) for i in range(4)]
        tj = {job: i for i, job in enumerate(tjobs)}

        def drow_at(g):
            return 0 if g == 0 else GRP * GRP * g - LEAD - 1

        block = ctx.enter_context(nc.Block())

        @block.sync
        def _(sp):
            sp.dma_start(w_raw, w).then_inc(w_in, 16)
            for n in range(T):
                sp.dma_start(S[:, n, :], adj_v[n]).then_inc(adj_in[n], 16)
            sp.wait_ge(w_ready, 1)
            for e in range(2):
                sp.dma_start(xres[:, e, :].rearrange("p (b f) -> p b f", b=GRP),
                             x_v[0, e]).then_inc(res_in[e], 16)
            for e in range(NEPI):
                s = e % 2
                sp.wait_ge(res_ready, e + 1)
                sp.dma_start(out_v[e // T, e % T],
                             res[:, s, :].rearrange("p (b f) -> p b f", b=GRP)).then_inc(out_done[s], 16)
                if e + 2 < NEPI:
                    sp.dma_start(xres[:, s, :].rearrange("p (b f) -> p b f", b=GRP),
                                 x_v[(e + 2) // T, (e + 2) % T]).then_inc(res_in[s], 16)
            for s in range(2):
                sp.wait_ge(out_done[s], 16 * (NEPI // 2))

        def load_x(act, u):
            act.dma_start(xin[:, u % X_SLOTS, :].rearrange("p (b f) -> p b f", b=GRP),
                          x_v[u // T, u % T]).then_inc(x_in[u % X_SLOTS], 16)

        @block.gpsimd
        def _(pool):
            nc.gpsimd.memset(ident[:], 0.0).then_inc(ident_zero, 1)
            nc.gpsimd.memset(mhalf[:], -0.5).then_inc(ident_zero, 1)
            pool.wait_ge(ident_zero, 2)
            nc.gpsimd.affine_select(out=ident[:], in_=ident[:], compare_op=ALU.not_equal, fill=1.0, base=0,
                                    pattern=[[-1, P]], channel_multiplier=1).then_inc(ident_ready, 1)
            chain = [0]

            def link(ins):
                chain[0] += 1
                ins.then_inc(ln_chain, 1)
                pool.wait_ge(ln_chain, chain[0])

            def inv_sqrt(v, y, t, c):
                link(nc.gpsimd.tensor_tensor(y, v, c, ALU.pow))
                link(nc.gpsimd.tensor_tensor(t, v, y, ALU.mult))
                link(nc.gpsimd.tensor_tensor(t, t, y, ALU.mult))
                link(nc.gpsimd.tensor_scalar(t, t, -0.5, 1.5, ALU.mult, ALU.add))

            def normalise(u):
                s = u % 2
                neg_mean, v, y, t = (lnt[:, s, i, :] for i in range(4))
                pool.wait_ge(stats_ready, u + 1)
                link(nc.gpsimd.tensor_scalar(neg_mean, mv[:, s, :, 0], -1.0, 0.0, ALU.mult, ALU.add))
                link(nc.gpsimd.tensor_scalar(v, mv[:, s, :, 1], 1.0, EPS, ALU.mult, ALU.add))
                inv_sqrt(v, y, t, mhalf[:, 0:GRP])
                link(nc.gpsimd.tensor_tensor(y, y, t, ALU.mult))
                for b in range(GRP):
                    xs = xin[:, u % X_SLOTS, b * P:(b + 1) * P]
                    last = nc.gpsimd.tensor_scalar(xs, xs, neg_mean[:, b:b + 1], y[:, b:b + 1], ALU.add, ALU.mult)
                last.then_inc(xn_ready, 1)

            for u in range(T):
                normalise(u)

            D, none, safe, y, t, some = (deg[:, i, :] for i in range(6))
            pool.wait_ge(deg_summed, 1)
            link(nc.gpsimd.tensor_scalar(none, D, 0.0, None, ALU.is_le))
            link(nc.gpsimd.tensor_scalar(some, D, 0.0, None, ALU.is_gt))
            link(nc.gpsimd.tensor_tensor(safe, D, none, ALU.add))
            inv_sqrt(safe, y, t, mhalf[:])
            link(nc.gpsimd.tensor_tensor(y, y, some, ALU.mult))
            link(nc.gpsimd.tensor_tensor(dcol[:], y, t, ALU.mult))
            nc.gpsimd.tensor_scalar(ndcol[:], dcol[:], -L_SCALE, 0.0, ALU.mult, ALU.add).then_inc(d_ready, 1)

            def add_x(e):
                s = e % 2
                pool.wait_ge(prod_taken, e + 1)
                pool.wait_ge(res_in[s], 16 * (e // 2 + 1))
                nc.gpsimd.tensor_tensor(res[:, s, :], res[:, s, :], xres[:, s, :], ALU.add).then_inc(res_ready, 1)

            for g in range(G):
                for i in range(GRP):
                    normalise(T + GRP * g + i)
                    if g and i == 0:
                        for nb in range(GRP):
                            add_x(GRP * (g - 1) + nb)
            for e in range(GRP * (G - 1), NEPI):
                add_x(e)

        @block.scalar
        def _(act):
            for u in range(X_SLOTS):
                load_x(act, u)

            def take_hT(u):
                act.wait_ge(t_turned, tj[("x", u)] + 1)
                if u >= 2:
                    act.wait_ge(hw_done, u - 1)
                nc.scalar.activation(hT[:, u % 2, :], ps[:, 4 + tj[("x", u)] % 2, :], ACT.Relu).then_inc(t_taken, 1)
                if u + X_SLOTS < HALVES * T:
                    load_x(act, u + X_SLOTS)

            def split_hw_hi(u):
                act.wait_ge(hw_done, u + 1)
                nc.scalar.activation(hw_hi[:, u // T, u % T, :], ps[:, 6 + u % 2, :],
                                     ACT.Copy).then_inc(hw_hi_ready, 1)

            units = list(relu_units)
            for n in range(T):
                while units and units[0][0] == n:
                    _, mt, g, adds = units.pop(0)
                    act.wait_ge(a_added, adds)
                    piece = S[:, mt, g * WIDE:(g + 1) * WIDE]
                    nc.scalar.activation(piece, piece, ACT.Relu,
                                         accum_out=deg_part[:, mt, g:g + 1]).then_inc(unit_relu, 1)
                for u in xunits_after_row[n]:
                    take_hT(u)
                    if u:
                        split_hw_hi(u - 1)
            split_hw_hi(T - 1)

            def take_drow(g):
                act.wait_ge(t_turned, tj[("drow", g)] + 1)
                if g:
                    act.wait_ge(l_scaled, T * g)
                nc.scalar.activation(drow[:], ps[:, 4 + tj[("drow", g)] % 2, :], ACT.Copy).then_inc(t_taken, 1)

            def split_l_hi(t):
                g, mt = t // T, t % T
                act.wait_ge(l_scaled, t + 1)
                nc.scalar.activation(L16[:, mt, 2 * g * WIDE:(2 * g + 1) * WIDE], tmp[:, t % TMP_SLOTS, :],
                                     ACT.Copy).then_inc(l_hi_ready, 1)

            take_drow(0)
            for t in range(LEAD):
                split_l_hi(t)
            for tau in range(G * T):
                v = tau // 4
                if tau % 4 == 0:
                    take_hT(T + v)
                for g in range(1, G):
                    if tau == drow_at(g):
                        take_drow(g)
                if tau % 4 == 2:
                    split_hw_hi(T + v)
                if tau + LEAD < G * T:
                    split_l_hi(tau + LEAD)

        @block.vector
        def _(dve):
            nc.vector.memset(ones, 1.0).then_inc(w_chain, 1)
            dve.wait_ge(w_in, 16)
            nc.vector.scalar_tensor_tensor(w_abs, w_raw, -1.0, w_raw, ALU.mult, ALU.max).then_inc(w_chain, 1)
            dve.wait_ge(w_summed, 1)
            nc.vector.tensor_scalar(w_sum, ps[:, 6, 0:P], 1e-30, None, ALU.max).then_inc(w_chain, 1)
            dve.wait_ge(w_chain, 3)
            nc.vector.tensor_scalar(w_sum.bitcast(U32), w_sum.bitcast(U32), 0x7F800000, None,
                                    ALU.bitwise_and).then_inc(w_chain, 1)
            dve.wait_ge(w_chain, 4)
            nc.vector.reciprocal(w_inv, w_sum).then_inc(w_chain, 1)
            nc.vector.tensor_scalar(svec[:], w_sum, 1.0 / (L_SCALE * H_SCALE), None, ALU.mult)
            dve.wait_ge(w_chain, 5)
            nc.vector.scalar_tensor_tensor(w_sb[:], w_raw, H_SCALE, w_inv, ALU.mult, ALU.mult).then_inc(w_chain, 1)
            dve.wait_ge(w_chain, 6)
            dve.wait_ge(ident_ready, 1)
            nc.vector.tensor_scalar(ident_s[:], ident[:], L_SCALE, None, ALU.mult).then_inc(w_ready, 1)

            def statistics(u):
                s = u % 2
                dve.wait_ge(x_in[u % X_SLOTS], 16 * (u // X_SLOTS + 1))
                if u >= 2:
                    dve.wait_ge(xn_ready, u - 1)
                for b in range(GRP):
                    nc.vector.bn_stats(stats[:, s, b, :],
                                       xin[:, u % X_SLOTS, b * P:(b + 1) * P]).then_inc(stats_raw, 1)
                for b in range(GRP):
                    dve.wait_ge(stats_raw, GRP * u + b + 1)
                    last = nc.vector.bn_aggr(mv[:, s, b, :], stats[:, s, b, :])
                last.then_inc(stats_ready, 1)

            def split_hw_lo(u):
                dve.wait_ge(hw_hi_ready, u + 1)
                nc.vector.tensor_tensor(hw_lo[:, u // T, u % T, :], ps[:, 6 + u % 2, :],
                                        hw_hi[:, u // T, u % T, :], ALU.subtract).then_inc(hw_lo_ready, 1)

            def add_transposed(j):
                kind, a, b = jobs[j]
                bank = 2 * (j % 2)
                dve.wait_ge(a_turned, j + 1 if kind == "pair" else j + 2 - b)
                if kind == "pair":
                    row = S[:, a, b * WIDE:(b + 1) * WIDE]
                    col = S[:, GRP * b:GRP * (b + 1), a * P:(a + 1) * P]
                    nc.vector.tensor_tensor(row, ps[:, bank, :], row, ALU.add).then_inc(a_added, 1)
                    nc.vector.tensor_tensor(col, ps[:, bank + 1, :].rearrange("p (k c) -> p k c", k=GRP), col,
                                            ALU.add).then_inc(a_added, 1)
                else:
                    for i in range(2):
                        row = S[:, GRP * a + 2 * b + i, a * WIDE:(a + 1) * WIDE]
                        nc.vector.tensor_tensor(row, ps[:, bank + i, :], row, ALU.add).then_inc(a_added, 1)

            statistics(0)
            for n in range(T):
                for j in jobs_of_row[n]:
                    add_transposed(j)
                for u in xunits_after_row[n]:
                    statistics(u + 1)
                    if u:
                        split_hw_lo(u - 1)
            dve.wait_ge(unit_relu, n_units)
            nc.vector.reduce_sum(deg[:, 0, :], deg_part[:], AX_X).then_inc(deg_summed, 1)
            split_hw_lo(T - 1)

            def scale_l(t):
                g, mt = t // T, t % T
                slot = tmp[:, t % TMP_SLOTS, :]
                if mt == 0:
                    dve.wait_ge(t_taken, tj[("drow", g)] + 1)
                if t >= TMP_SLOTS:
                    dve.wait_ge(l_lo_ready, t - TMP_SLOTS + 1)
                ins = nc.vector.scalar_tensor_tensor(slot, S[:, mt, g * WIDE:(g + 1) * WIDE], ndcol[:, mt:mt + 1],
                                                     drow[:], ALU.mult, ALU.mult)
                if mt // GRP == g:
                    ins.then_inc(l_diag, 1)
                    dve.wait_ge(l_diag, mt + 1)
                    d = slot[:, (mt % GRP) * P:(mt % GRP + 1) * P]
                    ins = nc.vector.tensor_tensor(d, d, ident_s[:], ALU.add)
                ins.then_inc(l_scaled, 1)

            def split_l_lo(t):
                g, mt = t // T, t % T
                dve.wait_ge(l_hi_ready, t + 1)
                nc.vector.tensor_tensor(L16[:, mt, (2 * g + 1) * WIDE:(2 * g + 2) * WIDE], tmp[:, t % TMP_SLOTS, :],
                                        L16[:, mt, 2 * g * WIDE:(2 * g + 1) * WIDE],
                                        ALU.subtract).then_inc(l_lo_ready, 1)

            def take_product(e):
                s = e % 2
                dve.wait_ge(prod_done, e + 1)
                if e >= 2:
                    dve.wait_ge(out_done[s], 16 * (e // 2))
                nc.vector.scalar_tensor_tensor(
                    res[:, s, :].rearrange("p (b f) -> p b f", b=GRP),
                    ps[:, e % GRP, :].rearrange("p (b f) -> p b f", b=GRP), 0.0,
                    svec[:].unsqueeze(1).to_broadcast([P, GRP, P]), ALU.max, ALU.mult).then_inc(prod_taken, 1)

            dve.wait_ge(d_ready, 1)
            scale_l(0)
            for t in range(LEAD):
                scale_l(t + 1)
                split_l_lo(t)
            for tau in range(G * T):
                if tau % T == 0 and tau:
                    for nb in range(GRP):
                        take_product(GRP * (tau // T - 1) + nb)
                if tau + LEAD + 1 < G * T:
                    scale_l(tau + LEAD + 1)
                if tau + LEAD < G * T:
                    split_l_lo(tau + LEAD)
                v = tau // 4
                if tau % 4 == 1 and v + 1 < T:
                    statistics(T + v + 1)
                if tau % 4 == 2:
                    split_hw_lo(T + v)
            for e in range(GRP * (G - 1), NEPI):
                take_product(e)

        @block.tensor
        def _(pe):
            pe.wait_ge(w_chain, 2)
            nc.tensor.matmul(ps[:, 6, 0:P], ones, w_abs, start=True, stop=True).then_inc(w_summed, 1)
            pe.wait_ge(ident_ready, 1)

            def turn_adj(j):
                kind, a, b = jobs[j]
                bank = 2 * (j % 2)
                pe.wait_ge(adj_in[a if kind == "pair" else GRP * a + GRP - 1], 16)
                if j >= 2:
                    pe.wait_ge(a_added, 2 * (j - 1))
                for i in range(GRP if kind == "pair" else 2):
                    if kind == "pair":
                        nc.tensor.transpose(ps[:, bank, i * P:(i + 1) * P],
                                            S[:, GRP * b + i, a * P:(a + 1) * P], ident[:])
                        last = nc.tensor.transpose(ps[:, bank + 1, i * P:(i + 1) * P],
                                                   S[:, a, (GRP * b + i) * P:(GRP * b + i + 1) * P], ident[:])
                    else:
                        r = GRP * a + 2 * b + i
                        for k in range(GRP):
                            last = nc.tensor.transpose(ps[:, bank + i, k * P:(k + 1) * P],
                                                       S[:, GRP * a + k, r * P:(r + 1) * P], ident[:])
                last.then_inc(a_turned, 1)

            def turn(job):
                i = tj[job]
                if i >= 2:
                    pe.wait_ge(t_taken, i - 1)
                for k in range(GRP):
                    if job[0] == "x":
                        src = xin[:, job[1] % X_SLOTS, k * P:(k + 1) * P]
                    else:
                        src = dcol[:, GRP * job[1] + k:GRP * job[1] + k + 1].to_broadcast([P, P])
                    last = nc.tensor.transpose(ps[:, 4 + i % 2, k * P:(k + 1) * P], src, ident[:])
                last.then_inc(t_turned, 1)

            def turn_x(u):
                pe.wait_ge(xn_ready, u + 1)
                turn(("x", u))

            def multiply_w(u):
                pe.wait_ge(t_taken, tj[("x", u)] + 1)
                if u == 0:
                    pe.wait_ge(w_ready, 1)
                if u >= 2:
                    pe.wait_ge(hw_lo_ready, u - 1)
                for b in range(GRP):
                    last = nc.tensor.matmul(ps[:, 6 + u % 2, b * P:(b + 1) * P], hT[:, u % 2, b * P:(b + 1) * P],
                                            w_sb[:], start=True, stop=True)
                last.then_inc(hw_done, 1)

            for n in range(T):
                pe.wait_ge(adj_in[n], 16)
                for j in jobs_of_row[n]:
                    turn_adj(j)
                for u in xunits_after_row[n]:
                    turn_x(u)
                    if u:
                        multiply_w(u - 1)
            multiply_w(T - 1)
            pe.wait_ge(d_ready, 1)
            turn(("drow", 0))

            def products(g, half, mt, base):
                for nb in range(GRP):
                    if mt == 0 and not isinstance(base, int) or mt == 0 and base:
                        pe.wait_ge(prod_taken, base - GRP + nb + 1)
                    acc = ps[:, nb, :]
                    if isinstance(g, int):
                        hi = L16[:, mt, 2 * g * WIDE + nb * P:2 * g * WIDE + (nb + 1) * P]
                        lo = L16[:, mt, (2 * g + 1) * WIDE + nb * P:(2 * g + 1) * WIDE + (nb + 1) * P]
                    else:
                        hi = L16[:, mt, bass.ds(g * (2 * WIDE) + nb * P, P)]
                        lo = L16[:, mt, bass.ds(g * (2 * WIDE) + (WIDE + nb * P), P)]
                    nc.tensor.matmul(acc, hi, hw_hi[:, half, mt, :], start=(mt == 0), stop=False)
                    nc.tensor.matmul(acc, hi, hw_lo[:, half, mt, :], start=False, stop=False)
                    last = nc.tensor.matmul(acc, lo, hw_hi[:, half, mt, :], start=False, stop=(mt == T - 1))
                    if mt == T - 1:
                        last.then_inc(prod_done, 1)

            for tau in range(G * T):
                g, mt = tau // T, tau % T
                v = tau // 4
                if tau % 4 == 0:
                    turn_x(T + v)
                for gg in range(1, G):
                    if tau == drow_at(gg):
                        turn(("drow", gg))
                if tau % 4 == 2:
                    multiply_w(T + v)
                pe.wait_ge(l_lo_ready, tau + 1)
                if tau == 0:
                    pe.wait_ge(hw_lo_ready, T)
                products(g, 0, mt, GRP * g)
            pe.wait_ge(hw_lo_ready, HALVES * T)
            with pe.Fori(0, G) as g:
                for mt in range(T):
                    products(g, 1, mt, g * GRP + T)


_INS = ["x", "adj", "L0_gnn_W"]


def kernel(**inputs):
    import numpy as _np
    import concourse.bacc as _bacc
    from concourse import mybir as _mybir
    from concourse.bass_utils import run_bass_kernel_spmd as _run

    nc = _bacc.Bacc("TRN2", target_bir_lowering=False, num_devices=1, dynamic_dma_scratch_size=1024)
    arrays, args = {}, []
    for name in _INS:
        a = _np.ascontiguousarray(inputs[name])
        arrays[f"in_{name}_dram"] = a
        args.append(nc.dram_tensor(f"in_{name}_dram", a.shape, _mybir.dt.from_np(a.dtype), kind="ExternalInput").ap())
    x = arrays["in_x_dram"]
    out = nc.dram_tensor("out_0_dram", x.shape, _mybir.dt.from_np(x.dtype), kind="ExternalOutput").ap()
    gnn_layer(nc, *args, out)
    r = _run(nc, [arrays], core_ids=[0])
    return r.results[0]["out_0_dram"]
```

```python
from contextlib import ExitStack

import concourse.bass as bass
from concourse import mybir
from concourse.alu_op_type import AluOpType as ALU

F32 = mybir.dt.float32
F16 = mybir.dt.float16
U32 = mybir.dt.uint32
ACT = mybir.ActivationFunctionType
AX_X = mybir.AxisListType.X

P = 128
GRP = 4
WIDE = GRP * P
EPS = 1e-5
L_SCALE = 2.0 ** 14
H_SCALE = 2.0 ** 10
X_EARLY = 8
X_RING = 3
LN_SLOTS = 8
STATS_LEAD = 3
LN_OPS = 7
TMP_SLOTS = 2
LEAD = 3


def gnn_layer(nc, x, adj, w, out):
    B, N, F = x.shape
    T = N // P
    G = T // GRP
    HALVES = B // GRP
    STEPS = G * T
    assert (HALVES, F, w.shape[1]) == (2, P, P)

    jobs = []
    for n in range(T):
        for g in range(n // GRP):
            jobs.append(("pair", n, g))
        if n % GRP == GRP - 1:
            jobs += [("diag", n // GRP, 0), ("diag", n // GRP, 1)]
    jobs_of_row = [[j for j, job in enumerate(jobs)
                    if (job[1] if job[0] == "pair" else job[1] * GRP + GRP - 1) == n] for n in range(T)]
    relu_units = []
    for n in range(T):
        grp = n // GRP
        for j in jobs_of_row[n]:
            kind, a, b = jobs[j]
            if kind == "pair":
                relu_units.append((n, n, b, 2 * j + 1))
                if n % GRP == GRP - 1:
                    relu_units += [(n, GRP * b + i, grp, 2 * j + 2) for i in range(GRP)]
            else:
                relu_units += [(n, GRP * a + 2 * b + i, a, 2 * j + 1 + i) for i in range(2)]

    x_slot = [i // 2 for i in range(X_EARLY)]
    x_slot += [T + i for i in range(T - X_EARLY)]
    x_slot += [2 * T + (STEPS - T) * i // T for i in range(T)]
    drow_slot = [T] + [T + T * g - LEAD - 2 for g in range(1, G)]
    x_at = {}
    for u, slot in enumerate(x_slot):
        x_at.setdefault(slot, []).append(u)
    turned = []
    for slot in range(T + STEPS):
        turned += [("drow", g) for g in range(G) if drow_slot[g] == slot] + [("x", u) for u in x_at.get(slot, [])]
    turn_no = {job: i for i, job in enumerate(turned)}

    x_v = x.rearrange("(h b) (t p) f -> h t p b f", b=GRP, p=P)
    out_v = out.rearrange("(h b) (t p) f -> h t p b f", b=GRP, p=P)
    adj_v = adj.rearrange("(t p) m -> t p m", p=P)

    with ExitStack() as ctx:
        def sb(name, shape, dt=F32):
            return ctx.enter_context(nc.sbuf_tensor(name, shape, dt))

        def sem(name):
            return ctx.enter_context(nc.semaphore(name))

        S = sb("S", [P, T, N])
        L16 = S[:].bitcast(F16)
        hw_hi = sb("hw_hi", [P, HALVES, T, WIDE], F16)
        hw_lo = sb("hw_lo", [P, HALVES, T, WIDE], F16)
        x_ring = sb("x_ring", [P, X_RING, WIDE])
        hT = sb("hT", [P, 2, WIDE])
        tmp = sb("tmp", [P, TMP_SLOTS, WIDE])
        drow = sb("drow", [P, WIDE])
        sums = sb("sums", [P, GRP, WIDE])
        res = sb("res", [P, 2, WIDE])
        ident = sb("ident", [P, P])
        w_sb = sb("w_sb", [P, P])
        svec = sb("svec", [P, P])
        stats = sb("stats", [P, 2, GRP, 6])
        mv = sb("mv", [P, LN_SLOTS, GRP, 2])
        lnt = sb("lnt", [P, 2, 4, GRP])
        mhalf = sb("mhalf", [P, GRP])
        deg_part = sb("deg_part", [P, T, G])
        deg = sb("deg", [P, 6, T])
        dcol = sb("dcol", [P, T])
        ndcol = sb("ndcol", [P, T])
        ones, w_abs, w_raw, w_inv = (res[:, 0, i * P:(i + 1) * P] for i in range(4))
        w_sum = res[:, 1, 0:P]
        ps = ctx.enter_context(nc.psum_tensor("ps", [P, 8, WIDE], F32))

        early = [half16[:, 1].rearrange("p t w -> p (t w)").bitcast(F32) for half16 in (hw_hi, hw_lo)]

        def x_buf(u, b0=0, b1=GRP):
            if u < T:
                k = u % (T // 2)
                return early[u // (T // 2)][:, k * WIDE + b0 * P:k * WIDE + b1 * P]
            return x_ring[:, (u - T) % X_RING, b0 * P:b1 * P]

        adj_in = [sem(f"adj_in{n}") for n in range(T)]
        w_in = sem("w_in")
        x_early_in = [sem(f"x_early_in{u}") for u in range(T)]
        x_ring_in = [sem(f"x_ring_in{s}") for s in range(X_RING)]
        sums_in = [sem(f"sums_in{s}") for s in range(GRP)]
        out_done = [sem(f"out_done{s}") for s in range(GRP)]
        ident_zero = sem("ident_zero")
        ident_ready = sem("ident_ready")
        w_chain = sem("w_chain")
        w_summed = sem("w_summed")
        a_turned = sem("a_turned")
        a_added = sem("a_added")
        unit_relu = sem("unit_relu")
        deg_chain = sem("deg_chain")
        deg_safe = sem("deg_safe")
        deg_root = sem("deg_root")
        d_ready = sem("d_ready")
        stats_raw = sem("stats_raw")
        stats_ready = sem("stats_ready")
        ln_chain = sem("ln_chain")
        xn_ready = sem("xn_ready")
        t_turned = sem("t_turned")
        t_taken = sem("t_taken")
        hw_done = sem("hw_done")
        hw_hi_ready = sem("hw_hi_ready")
        hw_lo_ready = sem("hw_lo_ready")
        l_diag = sem("l_diag")
        l_scaled = sem("l_scaled")
        l_hi_ready = sem("l_hi_ready")
        l_lo_ready = sem("l_lo_ready")
        prod_done = sem("prod_done")
        prod_taken = sem("prod_taken")
        sum_ready = sem("sum_ready")

        def load_x(queue, u):
            done = x_early_in[u] if u < T else x_ring_in[(u - T) % X_RING]
            queue.dma_start(x_buf(u).rearrange("p (b f) -> p b f", b=GRP), x_v[u // T, u % T]).then_inc(done, 16)

        block = ctx.enter_context(nc.Block())

        @block.sync
        def _(sp):
            load_x(sp, 0)
            sp.dma_start(w_raw, w).then_inc(w_in, 16)
            for u in range(1, X_EARLY):
                load_x(sp, u)
            for n in range(T):
                sp.dma_start(S[:, n, :], adj_v[n]).then_inc(adj_in[n], 16)
            for u in range(X_EARLY, T + X_RING):
                load_x(sp, u)
            for half in range(HALVES):
                for g in range(G):
                    first = GRP * (half * G + g)
                    for nb in range(GRP):
                        if first:
                            sp.wait_ge(out_done[nb], 4 * first)
                        sp.dma_start(sums[:, nb, :].rearrange("p (b f) -> p b f", b=GRP),
                                     x_v[half, GRP * g + nb]).then_inc(sums_in[nb], 16)
                    for nb in range(GRP):
                        sp.wait_ge(sum_ready, first + nb + 1)
                        sp.dma_start(out_v[half, GRP * g + nb],
                                     sums[:, nb, :].rearrange("p (b f) -> p b f", b=GRP)).then_inc(out_done[nb], 16)
            for nb in range(GRP):
                sp.wait_ge(out_done[nb], 16 * HALVES * G)

        @block.gpsimd
        def _(pool):
            nc.gpsimd.memset(ident[:], 0.0).then_inc(ident_zero, 1)
            nc.gpsimd.memset(mhalf[:], -0.5).then_inc(ident_zero, 1)
            pool.wait_ge(ident_zero, 2)
            nc.gpsimd.affine_select(out=ident[:], in_=ident[:], compare_op=ALU.not_equal, fill=1.0, base=0,
                                    pattern=[[-1, P]], channel_multiplier=1).then_inc(ident_ready, 1)
            for u in range(HALVES * T):
                neg_mean, v, y, t = (lnt[:, u % 2, i, :] for i in range(4))
                at = LN_OPS * u
                pool.wait_ge(stats_ready, u + 1)
                nc.gpsimd.tensor_scalar(v, mv[:, u % LN_SLOTS, :, 1], 1.0, EPS, ALU.mult, ALU.add).then_inc(ln_chain, 1)
                nc.gpsimd.tensor_scalar(neg_mean, mv[:, u % LN_SLOTS, :, 0], -1.0, 0.0, ALU.mult,
                                        ALU.add).then_inc(ln_chain, 1)
                pool.wait_ge(ln_chain, at + 1)
                nc.gpsimd.tensor_tensor(y, v, mhalf[:], ALU.pow).then_inc(ln_chain, 1)
                pool.wait_ge(ln_chain, at + 3)
                nc.gpsimd.tensor_tensor(t, v, y, ALU.mult).then_inc(ln_chain, 1)
                pool.wait_ge(ln_chain, at + 4)
                nc.gpsimd.tensor_tensor(t, t, y, ALU.mult).then_inc(ln_chain, 1)
                pool.wait_ge(ln_chain, at + 5)
                nc.gpsimd.tensor_scalar(t, t, -0.5, 1.5, ALU.mult, ALU.add).then_inc(ln_chain, 1)
                pool.wait_ge(ln_chain, at + 6)
                nc.gpsimd.tensor_tensor(y, y, t, ALU.mult).then_inc(ln_chain, 1)
                pool.wait_ge(ln_chain, at + 7)
                for b in range(GRP):
                    xs = x_buf(u, b, b + 1)
                    last = nc.gpsimd.tensor_scalar(xs, xs, neg_mean[:, b:b + 1], y[:, b:b + 1], ALU.add, ALU.mult)
                last.then_inc(xn_ready, 1)

        @block.scalar
        def _(act):
            def take_hT(u):
                act.wait_ge(t_turned, turn_no[("x", u)] + 1)
                if u >= 2:
                    act.wait_ge(hw_done, u - 1)
                nc.scalar.activation(hT[:, u % 2, :], ps[:, 4 + turn_no[("x", u)] % 2, :],
                                     ACT.Relu).then_inc(t_taken, 1)
                if T <= u < HALVES * T - X_RING:
                    load_x(act, u + X_RING)

            def take_drow(g):
                act.wait_ge(t_turned, turn_no[("drow", g)] + 1)
                if g:
                    act.wait_ge(l_scaled, T * g)
                nc.scalar.activation(drow[:], ps[:, 4 + turn_no[("drow", g)] % 2, :], ACT.Copy).then_inc(t_taken, 1)

            def split_hw_hi(u):
                act.wait_ge(hw_done, u + 1)
                nc.scalar.activation(hw_hi[:, u // T, u % T, :], ps[:, 6 + u % 2, :],
                                     ACT.Copy).then_inc(hw_hi_ready, 1)

            def split_l_hi(t):
                g, mt = t // T, t % T
                act.wait_ge(l_scaled, t + 1)
                nc.scalar.activation(L16[:, mt, 2 * g * WIDE:(2 * g + 1) * WIDE], tmp[:, t % TMP_SLOTS, :],
                                     ACT.Copy).then_inc(l_hi_ready, 1)

            def x_work(slot):
                for u in x_at.get(slot - 1, []):
                    split_hw_hi(u)
                for u in x_at.get(slot, []):
                    take_hT(u)

            act.wait_ge(ident_ready, 1)
            nc.scalar.activation(deg[:, 5, 0:1], ident[:, 0:1], ACT.Sqrt)
            for slot in range(T):
                for row, mt, g, adds in relu_units:
                    if row == slot:
                        act.wait_ge(a_added, adds)
                        piece = S[:, mt, g * WIDE:(g + 1) * WIDE]
                        nc.scalar.activation(piece, piece, ACT.Relu,
                                             accum_out=deg_part[:, mt, g:g + 1]).then_inc(unit_relu, 1)
                x_work(slot)
            act.wait_ge(deg_safe, 1)
            nc.scalar.activation(deg[:, 3, :], deg[:, 2, :], ACT.Sqrt).then_inc(deg_root, 1)
            for tau in range(STEPS):
                if tau == 0:
                    take_drow(0)
                    for t in range(LEAD):
                        split_l_hi(t)
                if tau + LEAD < STEPS:
                    split_l_hi(tau + LEAD)
                for g in range(1, G):
                    if drow_slot[g] == T + tau:
                        take_drow(g)
                x_work(T + tau)
            for u in x_at.get(T + STEPS - 1, []):
                split_hw_hi(u)

        @block.vector
        def _(dve):
            def statistics(u):
                if u < T:
                    dve.wait_ge(x_early_in[u], 16)
                else:
                    dve.wait_ge(x_ring_in[(u - T) % X_RING], 16 * ((u - T) // X_RING + 1))
                if u >= LN_SLOTS:
                    dve.wait_ge(xn_ready, u - LN_SLOTS + 1)
                for b in range(GRP):
                    nc.vector.bn_stats(stats[:, u % 2, b, :], x_buf(u, b, b + 1)).then_inc(stats_raw, 1)
                for b in range(GRP):
                    dve.wait_ge(stats_raw, GRP * u + b + 1)
                    last = nc.vector.bn_aggr(mv[:, u % LN_SLOTS, b, :], stats[:, u % 2, b, :])
                last.then_inc(stats_ready, 1)

            def split_hw_lo(u):
                dve.wait_ge(hw_hi_ready, u + 1)
                nc.vector.tensor_tensor(hw_lo[:, u // T, u % T, :], ps[:, 6 + u % 2, :],
                                        hw_hi[:, u // T, u % T, :], ALU.subtract).then_inc(hw_lo_ready, 1)

            def x_work(slot):
                for u in x_at.get(slot - 1, []):
                    split_hw_lo(u)
                for u in x_at.get(slot + STATS_LEAD, []):
                    statistics(u)

            def add_transposed(j):
                kind, a, b = jobs[j]
                bank = 2 * (j % 2)
                dve.wait_ge(a_turned, j + 1 if kind == "pair" else j + 2 - b)
                if kind == "pair":
                    row = S[:, a, b * WIDE:(b + 1) * WIDE]
                    col = S[:, GRP * b:GRP * (b + 1), a * P:(a + 1) * P]
                    nc.vector.tensor_tensor(row, ps[:, bank, :], row, ALU.add).then_inc(a_added, 1)
                    nc.vector.tensor_tensor(col, ps[:, bank + 1, :].rearrange("p (k c) -> p k c", k=GRP), col,
                                            ALU.add).then_inc(a_added, 1)
                else:
                    for i in range(2):
                        row = S[:, GRP * a + 2 * b + i, a * WIDE:(a + 1) * WIDE]
                        nc.vector.tensor_tensor(row, ps[:, bank + i, :], row, ALU.add).then_inc(a_added, 1)

            def scale_l(t):
                g, mt = t // T, t % T
                buf = tmp[:, t % TMP_SLOTS, :]
                if mt == 0:
                    dve.wait_ge(t_taken, turn_no[("drow", g)] + 1)
                if t >= TMP_SLOTS:
                    dve.wait_ge(l_lo_ready, t - TMP_SLOTS + 1)
                ins = nc.vector.scalar_tensor_tensor(buf, S[:, mt, g * WIDE:(g + 1) * WIDE], ndcol[:, mt:mt + 1],
                                                     drow[:], ALU.mult, ALU.mult)
                if mt // GRP == g:
                    ins.then_inc(l_diag, 1)
                    dve.wait_ge(l_diag, mt + 1)
                    d = buf[:, (mt % GRP) * P:(mt % GRP + 1) * P]
                    ins = nc.vector.scalar_tensor_tensor(d, ident[:], L_SCALE, d, ALU.mult, ALU.add)
                ins.then_inc(l_scaled, 1)

            def split_l_lo(t):
                g, mt = t // T, t % T
                dve.wait_ge(l_hi_ready, t + 1)
                nc.vector.tensor_tensor(L16[:, mt, (2 * g + 1) * WIDE:(2 * g + 2) * WIDE], tmp[:, t % TMP_SLOTS, :],
                                        L16[:, mt, 2 * g * WIDE:(2 * g + 1) * WIDE],
                                        ALU.subtract).then_inc(l_lo_ready, 1)

            def take_product(e):
                dve.wait_ge(prod_done, e + 1)
                if e >= 2:
                    dve.wait_ge(sum_ready, e - 1)
                nc.vector.scalar_tensor_tensor(
                    res[:, e % 2, :].rearrange("p (b f) -> p b f", b=GRP),
                    ps[:, e % GRP, :].rearrange("p (b f) -> p b f", b=GRP), 0.0,
                    svec[:].unsqueeze(1).to_broadcast([P, GRP, P]), ALU.max, ALU.mult).then_inc(prod_taken, 1)

            def add_x(e):
                dve.wait_ge(prod_taken, e + 1)
                dve.wait_ge(sums_in[e % GRP], 16 * (e // GRP + 1))
                nc.vector.tensor_tensor(sums[:, e % GRP, :], res[:, e % 2, :], sums[:, e % GRP, :],
                                        ALU.add).then_inc(sum_ready, 1)

            def finish_group(first):
                take_product(first)
                for nb in range(1, GRP):
                    take_product(first + nb)
                    add_x(first + nb - 1)
                add_x(first + GRP - 1)

            nc.vector.memset(ones, 1.0).then_inc(w_chain, 1)
            dve.wait_ge(w_in, 16)
            nc.vector.scalar_tensor_tensor(w_abs, w_raw, -1.0, w_raw, ALU.mult, ALU.max).then_inc(w_chain, 1)
            for slot in range(STATS_LEAD):
                for u in x_at.get(slot, []):
                    statistics(u)
            dve.wait_ge(w_summed, 1)
            nc.vector.tensor_scalar(w_sum, ps[:, 6, 0:P], 1e-30, None, ALU.max).then_inc(w_chain, 1)
            dve.wait_ge(w_chain, 3)
            nc.vector.tensor_scalar(w_sum.bitcast(U32), w_sum.bitcast(U32), 0x7F800000, None,
                                    ALU.bitwise_and).then_inc(w_chain, 1)
            dve.wait_ge(w_chain, 4)
            nc.vector.reciprocal(w_inv, w_sum).then_inc(w_chain, 1)
            nc.vector.tensor_scalar(svec[:], w_sum, 1.0 / (L_SCALE * H_SCALE), None, ALU.mult)
            dve.wait_ge(w_chain, 5)
            nc.vector.scalar_tensor_tensor(w_sb[:], w_raw, H_SCALE, w_inv, ALU.mult, ALU.mult).then_inc(w_chain, 1)

            for slot in range(T):
                for j in jobs_of_row[slot]:
                    add_transposed(j)
                x_work(slot)

            D, none, safe, root, y, t = (deg[:, i, :] for i in range(6))
            dve.wait_ge(unit_relu, len(relu_units))
            nc.vector.reduce_sum(D, deg_part[:], AX_X).then_inc(deg_chain, 1)
            dve.wait_ge(deg_chain, 1)
            nc.vector.tensor_scalar(none, D, 0.0, None, ALU.is_le).then_inc(deg_chain, 1)
            dve.wait_ge(deg_chain, 2)
            nc.vector.tensor_tensor(safe, D, none, ALU.add).then_inc(deg_safe, 1)
            dve.wait_ge(deg_root, 1)
            nc.vector.reciprocal(y, root).then_inc(deg_chain, 1)
            dve.wait_ge(deg_chain, 3)
            nc.vector.tensor_tensor(t, safe, y, ALU.mult).then_inc(deg_chain, 1)
            dve.wait_ge(deg_chain, 4)
            nc.vector.tensor_tensor(t, t, y, ALU.mult).then_inc(deg_chain, 1)
            dve.wait_ge(deg_chain, 5)
            nc.vector.tensor_scalar(t, t, -0.5, 1.5, ALU.mult, ALU.add).then_inc(deg_chain, 1)
            nc.vector.tensor_scalar(none, D, 0.0, None, ALU.is_gt).then_inc(deg_chain, 1)
            dve.wait_ge(deg_chain, 6)
            nc.vector.tensor_tensor(y, y, t, ALU.mult).then_inc(deg_chain, 1)
            dve.wait_ge(deg_chain, 8)
            nc.vector.tensor_tensor(dcol[:], y, none, ALU.mult).then_inc(d_ready, 1)
            nc.vector.scalar_tensor_tensor(ndcol[:], y, -L_SCALE, none, ALU.mult, ALU.mult).then_inc(deg_chain, 1)
            dve.wait_ge(deg_chain, 9)

            for tau in range(STEPS):
                if tau == 0:
                    scale_l(0)
                    for t in range(LEAD):
                        scale_l(t + 1)
                        split_l_lo(t)
                elif tau % T == 0:
                    finish_group(GRP * (tau // T - 1))
                if tau + LEAD + 1 < STEPS:
                    scale_l(tau + LEAD + 1)
                if tau + LEAD < STEPS:
                    split_l_lo(tau + LEAD)
                x_work(T + tau)
            for u in x_at.get(T + STEPS - 1, []):
                split_hw_lo(u)
            for first in range(GRP * (G - 1), GRP * G * HALVES, GRP):
                finish_group(first)

        @block.tensor
        def _(pe):
            pe.wait_ge(w_chain, 2)
            nc.tensor.matmul(ps[:, 6, 0:P], ones, w_abs, start=True, stop=True).then_inc(w_summed, 1)
            pe.wait_ge(ident_ready, 1)

            def turn_adj(j):
                kind, a, b = jobs[j]
                bank = 2 * (j % 2)
                if j >= 2:
                    pe.wait_ge(a_added, 2 * (j - 1))
                for i in range(GRP if kind == "pair" else 2):
                    if kind == "pair":
                        nc.tensor.transpose(ps[:, bank, i * P:(i + 1) * P],
                                            S[:, GRP * b + i, a * P:(a + 1) * P], ident[:])
                        last = nc.tensor.transpose(ps[:, bank + 1, i * P:(i + 1) * P],
                                                   S[:, a, (GRP * b + i) * P:(GRP * b + i + 1) * P], ident[:])
                    else:
                        r = GRP * a + 2 * b + i
                        for k in range(GRP):
                            last = nc.tensor.transpose(ps[:, bank + i, k * P:(k + 1) * P],
                                                       S[:, GRP * a + k, r * P:(r + 1) * P], ident[:])
                last.then_inc(a_turned, 1)

            def turn(job):
                i = turn_no[job]
                if i >= 2:
                    pe.wait_ge(t_taken, i - 1)
                for k in range(GRP):
                    if job[0] == "x":
                        src = x_buf(job[1], k, k + 1)
                    else:
                        src = dcol[:, GRP * job[1] + k:GRP * job[1] + k + 1].to_broadcast([P, P])
                    last = nc.tensor.transpose(ps[:, 4 + i % 2, k * P:(k + 1) * P], src, ident[:])
                last.then_inc(t_turned, 1)

            def multiply_w(u):
                pe.wait_ge(t_taken, turn_no[("x", u)] + 1)
                if u == 0:
                    pe.wait_ge(w_chain, 6)
                if u >= 2:
                    pe.wait_ge(hw_lo_ready, u - 1)
                for b in range(GRP):
                    last = nc.tensor.matmul(ps[:, 6 + u % 2, b * P:(b + 1) * P], hT[:, u % 2, b * P:(b + 1) * P],
                                            w_sb[:], start=True, stop=True)
                last.then_inc(hw_done, 1)

            def x_work(slot):
                for u in x_at.get(slot - 1, []):
                    multiply_w(u)
                for u in x_at.get(slot, []):
                    pe.wait_ge(xn_ready, u + 1)
                    turn(("x", u))

            rows_in = 0
            for slot in range(T):
                if jobs_of_row[slot]:
                    for n in range(rows_in, slot + 1):
                        pe.wait_ge(adj_in[n], 16)
                    rows_in = slot + 1
                for j in jobs_of_row[slot]:
                    turn_adj(j)
                x_work(slot)

            def products(g, half, mt, taken):
                for nb in range(GRP):
                    if mt == 0 and taken is not None:
                        pe.wait_ge(prod_taken, taken + nb + 1)
                    acc = ps[:, nb, :]
                    hi, lo = (L16[:, mt, bass.ds(g * (2 * WIDE) + part * WIDE + nb * P, P)] for part in (0, 1))
                    nc.tensor.matmul(acc, hi, hw_hi[:, half, mt, :], start=(mt == 0), stop=False)
                    nc.tensor.matmul(acc, hi, hw_lo[:, half, mt, :], start=False, stop=False)
                    last = nc.tensor.matmul(acc, lo, hw_hi[:, half, mt, :], start=False, stop=(mt == T - 1))
                    if mt == T - 1:
                        last.then_inc(prod_done, 1)

            for tau in range(STEPS):
                g, mt = tau // T, tau % T
                for gg in range(G):
                    if drow_slot[gg] == T + tau:
                        if gg == 0:
                            pe.wait_ge(d_ready, 1)
                        turn(("drow", gg))
                x_work(T + tau)
                pe.wait_ge(l_lo_ready, tau + 1)
                if g == 0:
                    pe.wait_ge(hw_lo_ready, mt + 1)
                products(g, 0, mt, GRP * (g - 1) if g else None)
            for u in x_at.get(T + STEPS - 1, []):
                multiply_w(u)
            pe.wait_ge(hw_lo_ready, HALVES * T)
            with pe.Fori(0, G) as g:
                for mt in range(T):
                    products(g, 1, mt, g * GRP + GRP * (G - 1))


_INS = ["x", "adj", "L0_gnn_W"]


def kernel(**inputs):
    import numpy as _np
    import concourse.bacc as _bacc
    from concourse import mybir as _mybir
    from concourse.bass_utils import run_bass_kernel_spmd as _run

    nc = _bacc.Bacc("TRN2", target_bir_lowering=False, num_devices=1, dynamic_dma_scratch_size=1024)
    arrays, args = {}, []
    for name in _INS:
        a = _np.ascontiguousarray(inputs[name])
        arrays[f"in_{name}_dram"] = a
        args.append(nc.dram_tensor(f"in_{name}_dram", a.shape, _mybir.dt.from_np(a.dtype), kind="ExternalInput").ap())
    x = arrays["in_x_dram"]
    out = nc.dram_tensor("out_0_dram", x.shape, _mybir.dt.from_np(x.dtype), kind="ExternalOutput").ap()
    gnn_layer(nc, *args, out)
    r = _run(nc, [arrays], core_ids=[0])
    return r.results[0]["out_0_dram"]
```

```python
from contextlib import ExitStack

import concourse.bass as bass
from concourse import mybir
from concourse.alu_op_type import AluOpType as ALU

F32 = mybir.dt.float32
F16 = mybir.dt.float16
U32 = mybir.dt.uint32
ACT = mybir.ActivationFunctionType
AX_X = mybir.AxisListType.X

P = 128
GRP = 4
WIDE = GRP * P
EPS = 1e-5
L_SCALE = 2.0 ** 14
H_SCALE = 2.0 ** 10
X_EARLY_SLOTS = (0, 1, 2, 3, 4, 5)
X_EARLY = len(X_EARLY_SLOTS)
DVE_SUMMED = (0, 1, 3)
MIRROR_LAG = 3
LN_SLOTS = 6
STATS_LEAD = (3, 7)
HI_LEAD = 4
LO_LEAD = 4
LN_OPS = 7
TMP_SLOTS = 2
LEAD = 2


def gnn_layer(nc, x, adj, w, out):
    B, N, F = x.shape
    T = N // P
    G = T // GRP
    HALVES = B // GRP
    STEPS = G * T
    assert (HALVES, F, w.shape[1]) == (2, P, P)

    jobs = [(n, g, GRP if g < n // GRP else n % GRP + 1) for n in range(T) for g in range(n // GRP + 1)]
    mirrors = [j for j, (n, g, k) in enumerate(jobs) if n != GRP * g]
    mirror_no = {j: q for q, j in enumerate(mirrors)}
    mirror_blocks = [k - (n // GRP == g) for n, g, k in jobs]
    plan, pending = [[] for _ in range(T)], []
    for j, (n, g, _) in enumerate(jobs):
        plan[n].append(("job", j))
        if j in mirror_no:
            pending.append(j)
        if len(pending) > MIRROR_LAG:
            plan[n].append(("mirror", pending.pop(0)))
        if g == n // GRP:
            plan[n].append(("x", None))
    plan[T - 1] += [("mirror", j) for j in pending]

    x_slot = list(X_EARLY_SLOTS)
    x_slot += [T + i for i in range(T - X_EARLY)]
    x_slot += [2 * T + (STEPS - T) * i // T - (i < 1) for i in range(T)]
    drow_slot = [T] + [T + T * g - LEAD - 2 for g in range(1, G)]
    assert max(x_slot) + 2 < T + STEPS
    x_at = {}
    for u, slot in enumerate(x_slot):
        x_at.setdefault(slot, []).append(u)
    turned = []
    for slot in range(T + STEPS):
        turned += [("drow", g) for g in range(G) if drow_slot[g] == slot]
        turned += [("x", u) for u in x_at.get(slot, []) if u < T]
    turn_no = {job: i for i, job in enumerate(turned)}

    x_v = x.rearrange("(h b) (t p) f -> h t p b f", b=GRP, p=P)
    out_v = out.rearrange("(h b) (t p) f -> h t p b f", b=GRP, p=P)
    adj_v = adj.rearrange("(t p) m -> t p m", p=P)

    with ExitStack() as ctx:
        def sb(name, shape, dt=F32):
            return ctx.enter_context(nc.sbuf_tensor(name, shape, dt))

        def sem(name):
            return ctx.enter_context(nc.semaphore(name))

        S = sb("S", [P, T, N])
        L16 = S[:].bitcast(F16)
        hw_hi = sb("hw_hi", [P, HALVES, T, WIDE], F16)
        hw_lo = sb("hw_lo", [P, HALVES, T, WIDE], F16)
        ring = sb("ring", [P, 3, WIDE])
        hT = sb("hT", [P, 2, WIDE])
        tmp = sb("tmp", [P, TMP_SLOTS, WIDE])
        drow = sb("drow", [P, WIDE])
        sums = sb("sums", [P, GRP, WIDE])
        res = sb("res", [P, 2, WIDE])
        ident = sb("ident", [P, P])
        w_sb = sb("w_sb", [P, P])
        w16 = sb("w16", [P, 2, P], F16)
        svec = sb("svec", [P, P])
        stats = sb("stats", [P, 2, GRP, 6])
        mv = sb("mv", [P, LN_SLOTS, GRP, 2])
        lnt = sb("lnt", [P, 2, 4, GRP])
        mhalf = sb("mhalf", [P, GRP])
        dcol = sb("dcol", [P, T])
        ndcol = sb("ndcol", [P, T])
        ones, w_abs, w_raw, w_inv = (res[:, 0, i * P:(i + 1) * P] for i in range(4))
        w_sum = res[:, 1, 0:P]
        deg = res[:, 0, P:P + 6 * T].rearrange("p (i t) -> p i t", i=6)
        deg_part = res[:, 1, P:P + T * (G + T)].rearrange("p (t c) -> p t c", t=T)
        ps = ctx.enter_context(nc.psum_tensor("ps", [P, 8, WIDE], F32))

        early = [half16[:, 1].rearrange("p t w -> p (t w)").bitcast(F32) for half16 in (hw_hi, hw_lo)]

        def x_buf(u, b0=0, b1=GRP):
            if u < T:
                k = u % (T // 2)
                return early[u // (T // 2)][:, k * WIDE + b0 * P:k * WIDE + b1 * P]
            return ring[:, 2 * (u - T) % 3, b0 * P:b1 * P]

        def h16(u, part):
            return ring[:, (2 * (u - T) + 1) % 3, :].bitcast(F16)[:, part * WIDE:(part + 1) * WIDE]

        def hT16(u, part):
            return hT[:, u % 2, :].bitcast(F16)[:, part * WIDE:(part + 1) * WIDE]

        adj_in = [sem(f"adj_in{n}") for n in range(T)]
        w_in = sem("w_in")
        x_early_in = [sem(f"x_early_in{u}") for u in range(T)]
        x_ring_in = [sem(f"x_ring_in{s}") for s in range(2)]
        h_hi_ready = sem("h_hi_ready")
        h_lo_ready = sem("h_lo_ready")
        h_turned = sem("h_turned")
        sums_in = [sem(f"sums_in{s}") for s in range(GRP)]
        out_done = [sem(f"out_done{s}") for s in range(GRP)]
        ident_zero = sem("ident_zero")
        ident_ready = sem("ident_ready")
        w_chain = sem("w_chain")
        w_summed = sem("w_summed")
        a_turned = sem("a_turned")
        a_added = sem("a_added")
        s_ready = sem("s_ready")
        m_turned = sem("m_turned")
        m_taken = sem("m_taken")
        m_summed = sem("m_summed")
        zeroed = sem("zeroed")
        deg_chain = sem("deg_chain")
        deg_safe = sem("deg_safe")
        deg_root = sem("deg_root")
        d_ready = sem("d_ready")
        stats_raw = sem("stats_raw")
        stats_ready = sem("stats_ready")
        ln_chain = sem("ln_chain")
        xn_ready = sem("xn_ready")
        xn_dve = sem("xn_dve")
        t_turned = sem("t_turned")
        t_taken = sem("t_taken")
        hw_done = sem("hw_done")
        hw_hi_ready = sem("hw_hi_ready")
        hw_lo_ready = sem("hw_lo_ready")
        l_diag = sem("l_diag")
        l_scaled = sem("l_scaled")
        l_hi_ready = sem("l_hi_ready")
        l_lo_ready = sem("l_lo_ready")
        prod_done = sem("prod_done")
        prod_taken = sem("prod_taken")
        sum_ready = sem("sum_ready")

        def load_x(queue, u):
            done = x_early_in[u] if u < T else x_ring_in[u % 2]
            queue.dma_start(x_buf(u).rearrange("p (b f) -> p b f", b=GRP), x_v[u // T, u % T]).then_inc(done, 16)

        block = ctx.enter_context(nc.Block())

        @block.sync
        def _(sp):
            load_x(sp, 0)
            sp.dma_start(w_raw, w).then_inc(w_in, 16)
            for u in range(1, X_EARLY):
                load_x(sp, u)
            for n in range(T):
                sp.dma_start(S[:, n, :], adj_v[n]).then_inc(adj_in[n], 16)
            for u in range(X_EARLY, T + 2):
                load_x(sp, u)

            def load_sums(g):
                for nb in range(GRP):
                    if g:
                        sp.wait_ge(out_done[nb], 16 * g)
                    sp.dma_start(sums[:, nb, :].rearrange("p (b f) -> p b f", b=GRP),
                                 x_v[g // G, GRP * (g % G) + nb]).then_inc(sums_in[nb], 16)

            def store_sums(g):
                for nb in range(GRP):
                    sp.wait_ge(sum_ready, GRP * g + nb + 1)
                    sp.dma_start(out_v[g // G, GRP * (g % G) + nb],
                                 sums[:, nb, :].rearrange("p (b f) -> p b f", b=GRP)).then_inc(out_done[nb], 16)

            def turn_h(u):
                sp.wait_ge(hw_done, u - 1)
                sp.wait_ge(h_hi_ready, u - T + 1)
                sp.wait_ge(h_lo_ready, u - T + 1)
                for part in range(2):
                    n = 2 * (u - T) + part
                    if n:
                        sp.wait_ge(h_turned, 16 * n)
                    sp.dma_start_transpose(hT16(u, part).rearrange("p (b r) -> p b r", b=GRP),
                                           h16(u, part)).then_inc(h_turned, 16)
                if u + 2 < HALVES * T:
                    sp.wait_ge(h_turned, 16 * (n + 1))
                    load_x(sp, u + 2)

            load_sums(0)
            for slot in range(T, T + STEPS):
                for u in x_at.get(slot + LO_LEAD, []):
                    if u >= T:
                        turn_h(u)
                g = (slot - T) // T
                if g > 0 and (slot - T) % T == 6:
                    store_sums(g - 1)
                    load_sums(g)
            for g in range(G - 1, HALVES * G):
                store_sums(g)
                if g + 1 < HALVES * G:
                    load_sums(g + 1)
            for nb in range(GRP):
                sp.wait_ge(out_done[nb], 16 * HALVES * G)

        @block.gpsimd
        def _(pool):
            nc.gpsimd.memset(ident[:], 0.0).then_inc(ident_zero, 1)
            nc.gpsimd.memset(mhalf[:], -0.5).then_inc(ident_zero, 1)
            pool.wait_ge(ident_zero, 2)
            nc.gpsimd.affine_select(out=ident[:], in_=ident[:], compare_op=ALU.not_equal, fill=1.0, base=0,
                                    pattern=[[-1, P]], channel_multiplier=1).then_inc(ident_ready, 1)
            for u in range(HALVES * T):
                neg_mean, v, y, t = (lnt[:, u % 2, i, :] for i in range(4))
                at = LN_OPS * u
                pool.wait_ge(stats_ready, u + 1)
                if 2 <= u < X_EARLY + 2:
                    pool.wait_ge(xn_dve, u - 1)
                nc.gpsimd.tensor_scalar(v, mv[:, u % LN_SLOTS, :, 1], 1.0, EPS, ALU.mult, ALU.add).then_inc(ln_chain, 1)
                nc.gpsimd.tensor_scalar(neg_mean, mv[:, u % LN_SLOTS, :, 0], -1.0, 0.0, ALU.mult,
                                        ALU.add).then_inc(ln_chain, 1)
                pool.wait_ge(ln_chain, at + 1)
                nc.gpsimd.tensor_tensor(y, v, mhalf[:], ALU.pow).then_inc(ln_chain, 1)
                pool.wait_ge(ln_chain, at + 3)
                nc.gpsimd.tensor_tensor(t, v, y, ALU.mult).then_inc(ln_chain, 1)
                pool.wait_ge(ln_chain, at + 4)
                nc.gpsimd.tensor_tensor(t, t, y, ALU.mult).then_inc(ln_chain, 1)
                pool.wait_ge(ln_chain, at + 5)
                scale = 1.0 if u < T else H_SCALE
                nc.gpsimd.tensor_scalar(t, t, -0.5 * scale, 1.5 * scale, ALU.mult, ALU.add).then_inc(ln_chain, 1)
                pool.wait_ge(ln_chain, at + 6)
                nc.gpsimd.tensor_tensor(y, y, t, ALU.mult).then_inc(ln_chain, 1)
                pool.wait_ge(ln_chain, at + 7)
                for b in range(GRP // 2 if u < X_EARLY else 0, GRP):
                    xs = x_buf(u, b, b + 1)
                    last = nc.gpsimd.tensor_scalar(xs, xs, neg_mean[:, b:b + 1], y[:, b:b + 1], ALU.add, ALU.mult)
                last.then_inc(xn_ready, 1)

        @block.scalar
        def _(act):
            def take_hT(u):
                act.wait_ge(t_turned, turn_no[("x", u)] + 1)
                if u >= 2:
                    act.wait_ge(hw_done, u - 1)
                nc.scalar.activation(hT[:, u % 2, :], ps[:, 4 + turn_no[("x", u)] % 2, :],
                                     ACT.Relu).then_inc(t_taken, 1)

            def take_drow(g):
                act.wait_ge(t_turned, turn_no[("drow", g)] + 1)
                if g:
                    act.wait_ge(l_scaled, T * g)
                nc.scalar.activation(drow[:], ps[:, 4 + turn_no[("drow", g)] % 2, :], ACT.Copy).then_inc(t_taken, 1)

            def split_hw_hi(u):
                act.wait_ge(hw_done, u + 1)
                nc.scalar.activation(hw_hi[:, u // T, u % T, :], ps[:, 6 + u % 2, :], ACT.Copy,
                                     scale=1.0 if u < T else 1.0 / H_SCALE).then_inc(hw_hi_ready, 1)

            def split_l_hi(t):
                g, mt = t // T, t % T
                act.wait_ge(l_scaled, t + 1)
                nc.scalar.activation(L16[:, mt, 2 * g * WIDE:(2 * g + 1) * WIDE], tmp[:, t % TMP_SLOTS, :],
                                     ACT.Copy).then_inc(l_hi_ready, 1)

            def split_h_hi(u):
                act.wait_ge(xn_ready, u + 1)
                if u >= T + 2:
                    act.wait_ge(h_turned, 32 * (u - T - 1))
                if u > T:
                    act.wait_ge(h_lo_ready, u - T)
                nc.scalar.activation(h16(u, 0), x_buf(u), ACT.Relu).then_inc(h_hi_ready, 1)

            def x_work(slot):
                for u in x_at.get(slot - 1, []):
                    split_hw_hi(u)
                for u in x_at.get(slot, []):
                    if u < T:
                        take_hT(u)
                for u in x_at.get(slot + HI_LEAD, []):
                    if u >= T:
                        split_h_hi(u)

            act.wait_ge(ident_ready, 1)
            nc.scalar.activation(dcol[:, 0:1], ident[:, 0:1], ACT.Sqrt)

            def relu_s(j):
                n, g, k = jobs[j]
                act.wait_ge(a_added, j + 1)
                piece = S[:, n, g * WIDE:g * WIDE + k * P]
                nc.scalar.activation(piece, piece, ACT.Relu, accum_out=deg_part[:, n, g:g + 1]).then_inc(s_ready, 1)

            def take_mirror(j):
                n, g, _ = jobs[j]
                k, q = mirror_blocks[j], mirror_no[j]
                act.wait_ge(m_turned, q + 1)
                bank = ps[:, 2 * (q % 2) + 1, :]
                if g in DVE_SUMMED:
                    nc.scalar.activation(S[:, GRP * g:GRP * g + k, n * P:(n + 1) * P],
                                         bank[:, 0:k * P].rearrange("p (k c) -> p k c", k=k),
                                         ACT.Copy).then_inc(m_taken, 1)
                else:
                    for i in range(k):
                        last = nc.scalar.activation(S[:, GRP * g + i, n * P:(n + 1) * P], bank[:, i * P:(i + 1) * P],
                                                    ACT.Copy, accum_out=deg_part[:, GRP * g + i, G + n:G + n + 1])
                    last.then_inc(m_taken, 1)

            act.wait_ge(zeroed, 1)
            for slot in range(T):
                for what, j in plan[slot]:
                    if what == "job":
                        relu_s(j)
                    elif what == "mirror":
                        take_mirror(j)
                    else:
                        x_work(slot)
            act.wait_ge(deg_safe, 1)
            nc.scalar.activation(deg[:, 3, :], deg[:, 2, :], ACT.Sqrt).then_inc(deg_root, 1)
            for tau in range(STEPS):
                if tau == 0:
                    take_drow(0)
                    for t in range(LEAD):
                        split_l_hi(t)
                if tau + LEAD < STEPS:
                    split_l_hi(tau + LEAD)
                for g in range(1, G):
                    if drow_slot[g] == T + tau:
                        take_drow(g)
                x_work(T + tau)

        @block.vector
        def _(dve):
            def statistics(u):
                if u < T:
                    dve.wait_ge(x_early_in[u], 16)
                else:
                    dve.wait_ge(x_ring_in[u % 2], 16 * ((u - T) // 2 + 1))
                if u >= LN_SLOTS:
                    dve.wait_ge(xn_ready, u - LN_SLOTS + 1)
                for b in range(GRP):
                    nc.vector.bn_stats(stats[:, u % 2, b, :], x_buf(u, b, b + 1)).then_inc(stats_raw, 1)
                for b in range(GRP):
                    dve.wait_ge(stats_raw, GRP * u + b + 1)
                    last = nc.vector.bn_aggr(mv[:, u % LN_SLOTS, b, :], stats[:, u % 2, b, :])
                last.then_inc(stats_ready, 1)

            def normalise(u):
                dve.wait_ge(ln_chain, LN_OPS * (u + 1))
                for b in range(GRP // 2):
                    xs = x_buf(u, b, b + 1)
                    last = nc.vector.tensor_scalar(xs, xs, lnt[:, u % 2, 0, b:b + 1], lnt[:, u % 2, 2, b:b + 1],
                                                   ALU.add, ALU.mult)
                last.then_inc(xn_dve, 1)

            def split_hw_lo(u):
                dve.wait_ge(hw_hi_ready, u + 1)
                nc.vector.scalar_tensor_tensor(hw_lo[:, u // T, u % T, :], ps[:, 6 + u % 2, :],
                                               1.0 if u < T else 1.0 / H_SCALE, hw_hi[:, u // T, u % T, :],
                                               ALU.mult, ALU.subtract).then_inc(hw_lo_ready, 1)

            def split_h_lo(u):
                dve.wait_ge(h_hi_ready, u - T + 1)
                nc.vector.scalar_tensor_tensor(h16(u, 1), x_buf(u), 0.0, h16(u, 0), ALU.max,
                                               ALU.subtract).then_inc(h_lo_ready, 1)

            def x_work(slot):
                for u in x_at.get(slot - 2, []):
                    split_hw_lo(u)
                for u in x_at.get(slot + 1, []):
                    if u < X_EARLY:
                        normalise(u)
                for u in x_at.get(slot + LO_LEAD, []):
                    if u >= T:
                        split_h_lo(u)
                for lead, units in zip(STATS_LEAD, (range(T), range(T, HALVES * T))):
                    for u in x_at.get(slot + lead, []):
                        if u in units:
                            statistics(u)

            def add_transposed(j):
                n, g, k = jobs[j]
                dve.wait_ge(a_turned, j + 1)
                piece = S[:, n, g * WIDE:g * WIDE + k * P]
                nc.vector.tensor_tensor(piece, ps[:, 2 * (j % 2), 0:k * P], piece, ALU.add).then_inc(a_added, 1)

            def sum_mirror(j):
                n, g, _ = jobs[j]
                k = mirror_blocks[j]
                dve.wait_ge(m_taken, mirror_no[j] + 1)
                nc.vector.reduce_sum(deg_part[:, GRP * g:GRP * g + k, G + n],
                                     S[:, GRP * g:GRP * g + k, n * P:(n + 1) * P], AX_X).then_inc(m_summed, 1)

            def scale_l(t):
                g, mt = t // T, t % T
                buf = tmp[:, t % TMP_SLOTS, :]
                if mt == 0:
                    dve.wait_ge(t_taken, turn_no[("drow", g)] + 1)
                if t >= TMP_SLOTS:
                    dve.wait_ge(l_lo_ready, t - TMP_SLOTS + 1)
                ins = nc.vector.scalar_tensor_tensor(buf, S[:, mt, g * WIDE:(g + 1) * WIDE], ndcol[:, mt:mt + 1],
                                                     drow[:], ALU.mult, ALU.mult)
                if mt // GRP == g:
                    ins.then_inc(l_diag, 1)
                    dve.wait_ge(l_diag, mt + 1)
                    d = buf[:, (mt % GRP) * P:(mt % GRP + 1) * P]
                    ins = nc.vector.scalar_tensor_tensor(d, ident[:], L_SCALE, d, ALU.mult, ALU.add)
                ins.then_inc(l_scaled, 1)

            def split_l_lo(t):
                g, mt = t // T, t % T
                dve.wait_ge(l_hi_ready, t + 1)
                nc.vector.tensor_tensor(L16[:, mt, (2 * g + 1) * WIDE:(2 * g + 2) * WIDE], tmp[:, t % TMP_SLOTS, :],
                                        L16[:, mt, 2 * g * WIDE:(2 * g + 1) * WIDE],
                                        ALU.subtract).then_inc(l_lo_ready, 1)

            def take_product(e):
                dve.wait_ge(prod_done, e + 1)
                if e >= 2:
                    dve.wait_ge(sum_ready, e - 1)
                nc.vector.scalar_tensor_tensor(
                    res[:, e % 2, :].rearrange("p (b f) -> p b f", b=GRP),
                    ps[:, e % GRP, :].rearrange("p (b f) -> p b f", b=GRP), 0.0,
                    svec[:].unsqueeze(1).to_broadcast([P, GRP, P]), ALU.max, ALU.mult).then_inc(prod_taken, 1)

            def add_x(e):
                dve.wait_ge(prod_taken, e + 1)
                dve.wait_ge(sums_in[e % GRP], 16 * (e // GRP + 1))
                nc.vector.tensor_tensor(sums[:, e % GRP, :], res[:, e % 2, :], sums[:, e % GRP, :],
                                        ALU.add).then_inc(sum_ready, 1)

            def take_group(first):
                take_product(first)
                take_product(first + 1)
                for e in range(first + 2, first + GRP):
                    add_x(e - 2)
                    take_product(e)

            def add_group_end(first):
                add_x(first + GRP - 2)
                add_x(first + GRP - 1)

            nc.vector.memset(ones, 1.0).then_inc(w_chain, 1)
            nc.vector.memset(deg_part, 0.0).then_inc(zeroed, 1)
            dve.wait_ge(w_in, 16)
            nc.vector.scalar_tensor_tensor(w_abs, w_raw, -1.0, w_raw, ALU.mult, ALU.max).then_inc(w_chain, 1)
            for slot in range(STATS_LEAD[0]):
                for u in x_at.get(slot, []):
                    statistics(u)
            for u in x_at.get(0, []):
                normalise(u)
            dve.wait_ge(w_summed, 1)
            nc.vector.tensor_scalar(w_sum, ps[:, 6, 0:P], 1e-30, None, ALU.max).then_inc(w_chain, 1)
            dve.wait_ge(w_chain, 3)
            nc.vector.tensor_scalar(w_sum.bitcast(U32), w_sum.bitcast(U32), 0x7F800000, None,
                                    ALU.bitwise_and).then_inc(w_chain, 1)
            dve.wait_ge(w_chain, 4)
            nc.vector.reciprocal(w_inv, w_sum).then_inc(w_chain, 1)
            nc.vector.tensor_scalar(svec[:], w_sum, 1.0 / (L_SCALE * H_SCALE), None, ALU.mult)
            dve.wait_ge(w_chain, 5)
            nc.vector.scalar_tensor_tensor(w_sb[:], w_raw, H_SCALE, w_inv, ALU.mult, ALU.mult).then_inc(w_chain, 1)
            dve.wait_ge(w_chain, 6)
            nc.vector.tensor_copy(w16[:, 0, :], w_sb[:]).then_inc(w_chain, 1)
            dve.wait_ge(w_chain, 7)
            nc.vector.tensor_tensor(w16[:, 1, :], w_sb[:], w16[:, 0, :], ALU.subtract).then_inc(w_chain, 1)

            dve_sums = [j for j in mirrors if jobs[j][1] in DVE_SUMMED]
            waiting = []
            for slot in range(T):
                for what, j in plan[slot]:
                    if what == "job":
                        add_transposed(j)
                    elif what == "x":
                        x_work(slot)
                    elif j in dve_sums:
                        waiting.append(j)
                    if len(waiting) > 1:
                        sum_mirror(waiting.pop(0))
            for j in waiting:
                sum_mirror(j)

            D, none, safe, root, y, t = (deg[:, i, :] for i in range(6))
            dve.wait_ge(s_ready, len(jobs))
            dve.wait_ge(m_taken, len(mirrors))
            dve.wait_ge(m_summed, len(dve_sums))
            nc.vector.reduce_sum(D, deg_part, AX_X).then_inc(deg_chain, 1)
            dve.wait_ge(deg_chain, 1)
            nc.vector.tensor_scalar(none, D, 0.0, None, ALU.is_le).then_inc(deg_chain, 1)
            dve.wait_ge(deg_chain, 2)
            nc.vector.tensor_tensor(safe, D, none, ALU.add).then_inc(deg_safe, 1)
            dve.wait_ge(deg_root, 1)
            nc.vector.reciprocal(y, root).then_inc(deg_chain, 1)
            dve.wait_ge(deg_chain, 3)
            nc.vector.tensor_tensor(t, safe, y, ALU.mult).then_inc(deg_chain, 1)
            dve.wait_ge(deg_chain, 4)
            nc.vector.tensor_tensor(t, t, y, ALU.mult).then_inc(deg_chain, 1)
            dve.wait_ge(deg_chain, 5)
            nc.vector.tensor_scalar(t, t, -0.5, 1.5, ALU.mult, ALU.add).then_inc(deg_chain, 1)
            nc.vector.tensor_scalar(none, D, 0.0, None, ALU.is_gt).then_inc(deg_chain, 1)
            dve.wait_ge(deg_chain, 6)
            nc.vector.tensor_tensor(y, y, t, ALU.mult).then_inc(deg_chain, 1)
            dve.wait_ge(deg_chain, 8)
            nc.vector.tensor_tensor(dcol[:], y, none, ALU.mult).then_inc(d_ready, 1)
            nc.vector.scalar_tensor_tensor(ndcol[:], y, -L_SCALE, none, ALU.mult, ALU.mult).then_inc(deg_chain, 1)
            dve.wait_ge(deg_chain, 9)

            for tau in range(STEPS):
                if tau == 0:
                    scale_l(0)
                    for t in range(LEAD):
                        scale_l(t + 1)
                        split_l_lo(t)
                elif tau % T == 0:
                    take_group(GRP * (tau // T - 1))
                if tau + LEAD + 1 < STEPS:
                    scale_l(tau + LEAD + 1)
                if tau + LEAD < STEPS:
                    split_l_lo(tau + LEAD)
                if tau and tau % T == 0:
                    add_group_end(GRP * (tau // T - 1))
                x_work(T + tau)
            for first in range(GRP * (G - 1), GRP * G * HALVES, GRP):
                take_group(first)
                add_group_end(first)

        @block.tensor
        def _(pe):
            pe.wait_ge(w_chain, 2)
            nc.tensor.matmul(ps[:, 6, 0:P], ones, w_abs, start=True, stop=True).then_inc(w_summed, 1)
            pe.wait_ge(ident_ready, 1)

            def turn_adj(j):
                n, g, k = jobs[j]
                if j >= 2:
                    pe.wait_ge(a_added, j - 1)
                for i in range(k):
                    last = nc.tensor.transpose(ps[:, 2 * (j % 2), i * P:(i + 1) * P],
                                               S[:, GRP * g + i, n * P:(n + 1) * P], ident[:])
                last.then_inc(a_turned, 1)

            def turn_mirror(j):
                n, g, _ = jobs[j]
                k, q = mirror_blocks[j], mirror_no[j]
                pe.wait_ge(s_ready, j + 1)
                if q >= 2:
                    pe.wait_ge(m_taken, q - 1)
                for i in range(k):
                    block = S[:, n, (GRP * g + i) * P:(GRP * g + i + 1) * P]
                    last = nc.tensor.transpose(ps[:, 2 * (q % 2) + 1, i * P:(i + 1) * P], block, ident[:])
                last.then_inc(m_turned, 1)

            def turn(job):
                i = turn_no[job]
                if i >= 2:
                    pe.wait_ge(t_taken, i - 1)
                for k in range(GRP):
                    if job[0] == "x":
                        src = x_buf(job[1], k, k + 1)
                    else:
                        src = dcol[:, GRP * job[1] + k:GRP * job[1] + k + 1].to_broadcast([P, P])
                    last = nc.tensor.transpose(ps[:, 4 + i % 2, k * P:(k + 1) * P], src, ident[:])
                last.then_inc(t_turned, 1)

            def multiply_w(u):
                if u < T:
                    pe.wait_ge(t_taken, turn_no[("x", u)] + 1)
                else:
                    pe.wait_ge(h_turned, 32 * (u - T + 1))
                if u == 0:
                    pe.wait_ge(w_chain, 6)
                if u == T:
                    pe.wait_ge(w_chain, 8)
                if u >= 2:
                    pe.wait_ge(hw_lo_ready, u - 1)
                for b in range(GRP):
                    acc, cols = ps[:, 6 + u % 2, b * P:(b + 1) * P], slice(b * P, (b + 1) * P)
                    if u < T:
                        last = nc.tensor.matmul(acc, hT[:, u % 2, cols], w_sb[:], start=True, stop=True)
                    else:
                        nc.tensor.matmul(acc, hT16(u, 0)[:, cols], w16[:, 0, :], start=True, stop=False)
                        nc.tensor.matmul(acc, hT16(u, 0)[:, cols], w16[:, 1, :], start=False, stop=False)
                        last = nc.tensor.matmul(acc, hT16(u, 1)[:, cols], w16[:, 0, :], start=False, stop=True)
                last.then_inc(hw_done, 1)

            def x_work(slot):
                for u in x_at.get(slot - 1, []):
                    if u < T:
                        multiply_w(u)
                for u in x_at.get(slot, []):
                    if u < T:
                        pe.wait_ge(xn_ready, u + 1)
                        if u < X_EARLY:
                            pe.wait_ge(xn_dve, u + 1)
                        turn(("x", u))
                    else:
                        multiply_w(u)

            for slot in range(T):
                pe.wait_ge(adj_in[slot], 16)
                for what, j in plan[slot]:
                    if what == "job":
                        turn_adj(j)
                    elif what == "mirror":
                        turn_mirror(j)
                    else:
                        x_work(slot)

            def products(g, half, mt, taken, blocks=range(GRP)):
                for nb in blocks:
                    if mt == 0 and taken is not None:
                        pe.wait_ge(prod_taken, taken + nb + 1)
                    acc = ps[:, nb, :]
                    hi, lo = (L16[:, mt, bass.ds(g * (2 * WIDE) + part * WIDE + nb * P, P)] for part in (0, 1))
                    nc.tensor.matmul(acc, hi, hw_hi[:, half, mt, :], start=(mt == 0), stop=False)
                    nc.tensor.matmul(acc, hi, hw_lo[:, half, mt, :], start=False, stop=False)
                    last = nc.tensor.matmul(acc, lo, hw_hi[:, half, mt, :], start=False, stop=(mt == T - 1))
                    if mt == T - 1:
                        last.then_inc(prod_done, 1)

            for tau in range(STEPS):
                g, mt = tau // T, tau % T
                for gg in range(G):
                    if drow_slot[gg] == T + tau:
                        if gg == 0:
                            pe.wait_ge(d_ready, 1)
                        turn(("drow", gg))
                x_work(T + tau)
                pe.wait_ge(l_lo_ready, tau + 1)
                if g == 0:
                    pe.wait_ge(hw_lo_ready, mt + 1)
                if g and mt == 0:
                    products(g, 0, 0, GRP * (g - 1), (0, 1))
                    pe.wait_ge(l_lo_ready, tau + 2)
                    products(g, 0, 1, None, (0, 1))
                    products(g, 0, 0, GRP * (g - 1), (2, 3))
                elif g and mt == 1:
                    products(g, 0, 1, None, (2, 3))
                else:
                    products(g, 0, mt, None)
            pe.wait_ge(hw_lo_ready, HALVES * T)
            with pe.Fori(0, G) as g:
                for nb in range(GRP):
                    for mt in range(T):
                        products(g, 1, mt, g * GRP + GRP * (G - 1), [nb])


_INS = ["x", "adj", "L0_gnn_W"]


def kernel(**inputs):
    import numpy as _np
    import concourse.bacc as _bacc
    from concourse import mybir as _mybir
    from concourse.bass_utils import run_bass_kernel_spmd as _run

    nc = _bacc.Bacc("TRN2", target_bir_lowering=False, num_devices=1, dynamic_dma_scratch_size=1024)
    arrays, args = {}, []
    for name in _INS:
        a = _np.ascontiguousarray(inputs[name])
        arrays[f"in_{name}_dram"] = a
        args.append(nc.dram_tensor(f"in_{name}_dram", a.shape, _mybir.dt.from_np(a.dtype), kind="ExternalInput").ap())
    x = arrays["in_x_dram"]
    out = nc.dram_tensor("out_0_dram", x.shape, _mybir.dt.from_np(x.dtype), kind="ExternalOutput").ap()
    gnn_layer(nc, *args, out)
    r = _run(nc, [arrays], core_ids=[0])
    return r.results[0]["out_0_dram"]
```
